# Optimizing a Trainium2 kernel written in Bass

```python
import numpy as np
import jax
import jax.numpy as jnp

def _softmax(x, axis=-1):
    return jax.nn.softmax(x, axis=axis)

def _gelu(x):
    return jax.nn.gelu(x, approximate=True)

def _silu(x):
    return jax.nn.silu(x)

def _sigmoid(x):
    return jax.nn.sigmoid(x)

def _layernorm(x, axis=-1, eps=1e-05):
    m = jnp.mean(x, axis=axis, keepdims=True)
    v = jnp.var(x, axis=axis, keepdims=True)
    return (x - m) / jnp.sqrt(v + eps)

def _scatter_add(tgt, idx, src, axis=0):
    return tgt.at[idx].add(src)

def _segment_sum(src, seg, n):
    return jax.ops.segment_sum(src, seg, n)
kernel_name = 'mk_seq_preln_d1_jaxref_r8_0ba1be'

def setup_inputs(seed: int=0):
    np.random.seed(seed)
    _w = jnp.asarray

    def _L0_attn_setup():
        import jax, jax.numpy as jnp
        import numpy as np
        LN_EPS = 1e-05
        WKV_EPS = 1e-08

        def _layernorm(x, g, b):
            mu = jnp.mean(x, axis=-1, keepdims=True)
            var = jnp.mean((x - mu) ** 2, axis=-1, keepdims=True)
            return (x - mu) * jax.lax.rsqrt(var + LN_EPS) * g + b

        def _time_mix(xn, Wr, Ww, Wk, Wv, Wo, time_decay):
            r = jax.nn.sigmoid(jnp.einsum('bsd,ed->bse', xn, Wr))
            w = -jnp.exp(jnp.einsum('bsd,ed->bse', xn, Ww))
            k = jnp.einsum('bsd,ed->bse', xn, Wk)
            v = jnp.einsum('bsd,ed->bse', xn, Wv)
            ewk = jnp.exp(w + k)
            decay = jnp.exp(time_decay)

            def step(carry, inp):
                num, den = carry
                e, vt = inp
                num = decay * num + e * vt
                den = decay * den + e
                wkv = num / (den + WKV_EPS)
                return ((num, den), wkv)
            B, S, D = xn.shape
            init = (jnp.zeros((B, D), xn.dtype), jnp.zeros((B, D), xn.dtype))
            (num_f, den_f), wkv = jax.lax.scan(step, init, (jnp.swapaxes(ewk, 0, 1), jnp.swapaxes(v, 0, 1)))
            wkv = jnp.swapaxes(wkv, 0, 1)
            out = jnp.einsum('bsd,ed->bse', r * wkv, Wo)
            final_state = jnp.stack([num_f, den_f], axis=1)
            return (out, final_state)

        def _channel_mix(xn, Wkey, Wval, Wrec):
            k = jnp.einsum('bsd,fd->bsf', xn, Wkey)
            k = jnp.square(jax.nn.relu(k))
            v = jnp.einsum('bsf,df->bsd', k, Wval)
            r = jax.nn.sigmoid(jnp.einsum('bsd,ed->bse', xn, Wrec))
            return r * v

        def _reference_tuple_inner(x, ln1_g, ln1_b, ln2_g, ln2_b, Wr, Ww, Wk, Wv, Wo, time_decay, time_first, Wkey, Wval, Wrec):
            tm, new_state = _time_mix(_layernorm(x, ln1_g, ln1_b), Wr, Ww, Wk, Wv, Wo, time_decay)
            x = x + tm
            x = x + _channel_mix(_layernorm(x, ln2_g, ln2_b), Wkey, Wval, Wrec)
            return (x, new_state)
        key = jax.random.key(seed)
        ks = jax.random.split(key, 16)
        B, S, D, F = (4, 256, 128, 512)
        xavier_d = float(np.sqrt(6.0 / (D + D)))
        xavier_df = float(np.sqrt(6.0 / (D + F)))
        u = lambda k, sh, s: jax.random.uniform(k, sh, jnp.float32, -s, s)
        return {'x': jax.random.normal(ks[0], (B, S, D), jnp.float32), 'ln1_g': jnp.ones((D,), jnp.float32), 'ln1_b': jnp.zeros((D,), jnp.float32), 'ln2_g': jnp.ones((D,), jnp.float32), 'ln2_b': jnp.zeros((D,), jnp.float32), 'Wr': u(ks[1], (D, D), xavier_d), 'Ww': u(ks[2], (D, D), xavier_d), 'Wk': u(ks[3], (D, D), xavier_d), 'Wv': u(ks[4], (D, D), xavier_d), 'Wo': u(ks[5], (D, D), xavier_d), 'time_decay': jax.random.uniform(ks[6], (D,), jnp.float32, -1.0, 0.0), 'time_first': jax.random.uniform(ks[7], (D,), jnp.float32, -1.0, 1.0), 'Wkey': u(ks[8], (F, D), xavier_df), 'Wval': u(ks[9], (D, F), xavier_df), 'Wrec': u(ks[10], (D, D), xavier_d)}
    _L0_attn_in = _L0_attn_setup()

    def _L0_ffn_setup():
        import jax, jax.numpy as jnp
        import numpy as np
        B, S, H = (2, 256, 128)
        N, F, SF, K = (16, 128, 512, 1)
        key = jax.random.key(seed)
        ks = jax.random.split(key, 7)
        std = 0.02
        return {'hidden_states': jax.random.normal(ks[0], (B, S, H), dtype=jnp.float32), 'router_w': jax.random.normal(ks[1], (N, H), dtype=jnp.float32) * std, 'gate_up_proj': jax.random.normal(ks[2], (N, H, 2 * F), dtype=jnp.float32) * std, 'down_proj': jax.random.normal(ks[3], (N, F, H), dtype=jnp.float32) * std, 'shared_gate_w': jax.random.normal(ks[4], (SF, H), dtype=jnp.float32) * std, 'shared_up_w': jax.random.normal(ks[5], (SF, H), dtype=jnp.float32) * std, 'shared_down_w': jax.random.normal(ks[6], (H, SF), dtype=jnp.float32) * std}
    _L0_ffn_in = _L0_ffn_setup()
    _d = {'L0_attn_x': _L0_attn_in['x'], 'L0_attn_ln1_g': _L0_attn_in['ln1_g'], 'L0_attn_ln1_b': _L0_attn_in['ln1_b'], 'L0_attn_ln2_g': _L0_attn_in['ln2_g'], 'L0_attn_ln2_b': _L0_attn_in['ln2_b'], 'L0_attn_Wr': _L0_attn_in['Wr'], 'L0_attn_Ww': _L0_attn_in['Ww'], 'L0_attn_Wk': _L0_attn_in['Wk'], 'L0_attn_Wv': _L0_attn_in['Wv'], 'L0_attn_Wo': _L0_attn_in['Wo'], 'L0_attn_time_decay': _L0_attn_in['time_decay'], 'L0_attn_time_first': _L0_attn_in['time_first'], 'L0_attn_Wkey': _L0_attn_in['Wkey'], 'L0_attn_Wval': _L0_attn_in['Wval'], 'L0_attn_Wrec': _L0_attn_in['Wrec'], 'L0_ffn_router_w': _L0_ffn_in['router_w'], 'L0_ffn_gate_up_proj': _L0_ffn_in['gate_up_proj'], 'L0_ffn_down_proj': _L0_ffn_in['down_proj'], 'L0_ffn_shared_gate_w': _L0_ffn_in['shared_gate_w'], 'L0_ffn_shared_up_w': _L0_ffn_in['shared_up_w'], 'L0_ffn_shared_down_w': _L0_ffn_in['shared_down_w']}
    _x0 = _d['L0_attn_x']
    _d['L0_attn_x'] = jax.random.normal(jax.random.fold_in(jax.random.key(seed), 1), (16, 512, 128), dtype=_x0.dtype)
    del _x0
    return _d

def reference(L0_attn_x, L0_attn_ln1_g, L0_attn_ln1_b, L0_attn_ln2_g, L0_attn_ln2_b, L0_attn_Wr, L0_attn_Ww, L0_attn_Wk, L0_attn_Wv, L0_attn_Wo, L0_attn_time_decay, L0_attn_time_first, L0_attn_Wkey, L0_attn_Wval, L0_attn_Wrec, L0_ffn_router_w, L0_ffn_gate_up_proj, L0_ffn_down_proj, L0_ffn_shared_gate_w, L0_ffn_shared_up_w, L0_ffn_shared_down_w):

    def _L0_attn_ref(x, ln1_g, ln1_b, ln2_g, ln2_b, Wr, Ww, Wk, Wv, Wo, time_decay, time_first, Wkey, Wval, Wrec):
        import jax, jax.numpy as jnp
        import numpy as np
        LN_EPS = 1e-05
        WKV_EPS = 1e-08

        def _layernorm(x, g, b):
            mu = jnp.mean(x, axis=-1, keepdims=True)
            var = jnp.mean((x - mu) ** 2, axis=-1, keepdims=True)
            return (x - mu) * jax.lax.rsqrt(var + LN_EPS) * g + b

        def _time_mix(xn, Wr, Ww, Wk, Wv, Wo, time_decay):
            r = jax.nn.sigmoid(jnp.einsum('bsd,ed->bse', xn, Wr))
            w = -jnp.exp(jnp.einsum('bsd,ed->bse', xn, Ww))
            k = jnp.einsum('bsd,ed->bse', xn, Wk)
            v = jnp.einsum('bsd,ed->bse', xn, Wv)
            ewk = jnp.exp(w + k)
            decay = jnp.exp(time_decay)

            def step(carry, inp):
                num, den = carry
                e, vt = inp
                num = decay * num + e * vt
                den = decay * den + e
                wkv = num / (den + WKV_EPS)
                return ((num, den), wkv)
            B, S, D = xn.shape
            init = (jnp.zeros((B, D), xn.dtype), jnp.zeros((B, D), xn.dtype))
            (num_f, den_f), wkv = jax.lax.scan(step, init, (jnp.swapaxes(ewk, 0, 1), jnp.swapaxes(v, 0, 1)))
            wkv = jnp.swapaxes(wkv, 0, 1)
            out = jnp.einsum('bsd,ed->bse', r * wkv, Wo)
            final_state = jnp.stack([num_f, den_f], axis=1)
            return (out, final_state)

        def _channel_mix(xn, Wkey, Wval, Wrec):
            k = jnp.einsum('bsd,fd->bsf', xn, Wkey)
            k = jnp.square(jax.nn.relu(k))
            v = jnp.einsum('bsf,df->bsd', k, Wval)
            r = jax.nn.sigmoid(jnp.einsum('bsd,ed->bse', xn, Wrec))
            return r * v

        def _reference_tuple_inner(x, ln1_g, ln1_b, ln2_g, ln2_b, Wr, Ww, Wk, Wv, Wo, time_decay, time_first, Wkey, Wval, Wrec):
            tm, new_state = _time_mix(_layernorm(x, ln1_g, ln1_b), Wr, Ww, Wk, Wv, Wo, time_decay)
            x = x + tm
            x = x + _channel_mix(_layernorm(x, ln2_g, ln2_b), Wkey, Wval, Wrec)
            return (x, new_state)
        return _reference_tuple_inner(x, ln1_g, ln1_b, ln2_g, ln2_b, Wr, Ww, Wk, Wv, Wo, time_decay, time_first, Wkey, Wval, Wrec)[0]

    def _L0_ffn_ref(hidden_states, router_w, gate_up_proj, down_proj, shared_gate_w, shared_up_w, shared_down_w):
        import jax, jax.numpy as jnp
        import numpy as np
        B, S, H = (2, 256, 128)
        N, F, SF, K = (16, 128, 512, 1)
        b, s, h = hidden_states.shape
        hidden = hidden_states.reshape(-1, h)
        t = hidden.shape[0]
        logits = hidden @ router_w.T
        top_vals, top_idx = jax.lax.top_k(logits, K)
        scores = jnp.full_like(logits, -jnp.inf)
        scores = scores.at[jnp.arange(t)[:, None], top_idx].set(top_vals)
        scores = jax.nn.sigmoid(scores.astype(jnp.float32)).astype(hidden.dtype)
        routed_in = hidden[None, :, :] * scores.T[:, :, None]
        gate_up = jnp.einsum('nth,nhf->ntf', routed_in, gate_up_proj)
        gate, up = jnp.split(gate_up, 2, axis=-1)
        routed_out = jnp.einsum('ntf,nfh->nth', up * jax.nn.silu(gate), down_proj)
        expert_sum = routed_out.sum(axis=0)
        shared = jax.nn.silu(hidden @ shared_gate_w.T) * (hidden @ shared_up_w.T) @ shared_down_w.T
        return (shared + expert_sum).reshape(b, s, h)
    x = L0_attn_x
    x = x + _L0_attn_ref(_layernorm(x, axis=-1), L0_attn_ln1_g, L0_attn_ln1_b, L0_attn_ln2_g, L0_attn_ln2_b, L0_attn_Wr, L0_attn_Ww, L0_attn_Wk, L0_attn_Wv, L0_attn_Wo, L0_attn_time_decay, L0_attn_time_first, L0_attn_Wkey, L0_attn_Wval, L0_attn_Wrec)
    x = x + _L0_ffn_ref(_layernorm(x, axis=-1), L0_ffn_router_w, L0_ffn_gate_up_proj, L0_ffn_down_proj, L0_ffn_shared_gate_w, L0_ffn_shared_up_w, L0_ffn_shared_down_w)
    return x

_drawn_inputs = setup_inputs


def setup_inputs(seed=0):
    import zlib

    import numpy as np

    out = dict(_drawn_inputs(seed))
    spreads = {'L0_attn_ln1_g': (1.0, 0.2),
     'L0_attn_ln1_b': (0.0, 0.287),
     'L0_attn_ln2_g': (1.0, 0.2),
     'L0_attn_ln2_b': (0.0, 0.343)}
    factors = {'L0_ffn_router_w': 8.0,
     'L0_ffn_gate_up_proj': 8.0,
     'L0_ffn_down_proj': 8.0,
     'L0_ffn_shared_gate_w': 8.0,
     'L0_ffn_shared_up_w': 8.0,
     'L0_ffn_shared_down_w': 8.0}
    for name, (base, spread) in spreads.items():
        noise = np.random.default_rng([zlib.crc32(name.encode()), seed]).standard_normal(out[name].shape)
        drawn = base * np.exp(spread * noise) if base else spread * noise
        out[name] = jnp.asarray(drawn.astype(out[name].dtype))
    for name, factor in factors.items():
        out[name] = (out[name] * factor).astype(out[name].dtype)
    return out
```

```python
from contextlib import ExitStack

import numpy as np
import concourse.bass as bass
from concourse import mybir

FP32 = mybir.dt.float32
BF16 = mybir.dt.bfloat16
I32 = mybir.dt.int32
U32 = mybir.dt.uint32
ALU = mybir.AluOpType
ACT = mybir.ActivationFunctionType
AX = mybir.AxisListType.X
PE_ENGINE, SP_ENGINE = mybir.EngineType.PE, mybir.EngineType.SP

P = 128
B, S, D = 16, 512, 128
F = 512
NE, EF, SF = 16, 128, 512
NTOK = B * S
T = S
G = T // P
NT = NTOK // T
LN_EPS, WKV_EPS = 1e-5, 1e-8
ROW = 2 * D + 1
REGION = NTOK + P
FILL_ROW = NE * REGION
NS = NTOK // P + NE
RING = 16
PACK = 4
EID_PAD = 6
WORDS = (NS + EID_PAD) // PACK + 2
NO_TOKEN = 1 << 20

MAIN = {}
_at = 0
for _n, _w in (("Ww", D), ("Wk", D), ("Wr", D), ("Wv", D), ("Wo", D), ("Wkey", F), ("Wrec", D), ("Wval", F),
               ("router", NE), ("gate", SF), ("up", SF), ("down", SF)):
    MAIN[_n] = (_at, _w)
    _at += _w
MAIN_COLS = _at
VEC = {n: i for i, n in enumerate(("g1", "b1", "g2", "b2", "decay"))}

PER = dict(
    statA=1, mvA=1, poolA=7, xn0=1, xn1tok=1, T1=1, xn1T=1,
    Wp=1, Kp=1, Rp=1, Vp=1, ew=1, z=1, e=1, E=1, ev=1, den=1, num=1, denp=1, q=1, rq=4, p=4,
    TM=1, a=1, statC=1, mvC=1, poolC=2, an=1, xa=1, T2=1, xn2T=1,
    KE=4, kr=4, k2=4, REC=1, th=1, VAL=1, rv=1, T3=1, x2=1,
    statE=1, mvE=1, poolE=2, h=1, T4=1, hT=1, LG=1, route=5, ths=1, sc=1, OS=3, RK=1, rank=5, hs=1, ids=2,
    Gp=4, Up=4, sg=4, act=4, DN=1, dn=1, T5=1, base=1,
    xT6=1, xhT=1, xGU=1, xsg=1, xact=1, xT7=1, xaT=1, xDN=1, xy=1,
)

SLOT_SEMS = ("xT6", "xhT", "xGU", "xsg", "xact", "xT7", "xaT", "xDN", "xy")


class InLoop:

    def __init__(self, register, step, at):
        self.register, self.step, self.at = register, step, at

    def __add__(self, k):
        return InLoop(self.register, self.step, self.at + k)

    def __sub__(self, k):
        return self + -k


def times(t, count, more=0):
    if isinstance(t, int):
        return t * count + more
    return t.register * (t.step * count) + (t.at * count + more)


def lap(t, m, count, more=0):
    if isinstance(t, int):
        return t // m * count + more
    assert t.step % m == 0
    return t.register * (t.step // m * count) + (t.at // m * count + more)


def program(nc, x, w_main, w_gu, w_down, vecs, out):
    sorted_rows = nc.dram_tensor("sorted_rows", [FILL_ROW + P, ROW], FP32)
    sorted_ap = sorted_rows.ap()
    x_tiles = x.rearrange("(t g p) d -> t p g d", p=P, g=G)

    with ExitStack() as ctx:
        def sb(name, cols, dt=FP32):
            return ctx.enter_context(nc.sbuf_tensor(name, [P] + (list(cols) if isinstance(cols, tuple) else [cols]), dt))

        def one(name, cols=T, dt=FP32):
            return [sb(name, cols, dt)] * 2

        def two(name, cols=T, dt=FP32):
            return [sb(f"{name}{i}", cols, dt) for i in range(2)]

        s = {n: ctx.enter_context(nc.semaphore(n)) for n in PER}
        for n in ("w_in0", "w_in1", "w_in2", "v_in", "x_in0", "x_in1", "xl_in0", "xl_in1", "scat0", "scat1", "fill_out",
                  "const_p", "const_d", "decay_s", "decay_d", "tab", "passed", *(f"{n}{i}" for n in ("xr_in", "xout") for i in range(RING))):
            s[n] = ctx.enter_context(nc.semaphore(n))

        def hold(eng, name, value):
            eng.wait_ge(s[name], value)
            if not isinstance(value, int) and eng in (nc.gpsimd, nc.sync):
                stand_alone(eng)

        def stand_alone(eng):
            eng.sem_inc(s["passed"], 1)

        def wait(eng, name, t, k=None):
            if isinstance(t, int):
                if t < 0:
                    return
                t = min(t, (NS if name in SLOT_SEMS else NT) - 1)
            hold(eng, name, times(t, PER[name], PER[name] if k is None else k))

        wm = sb("wm", MAIN_COLS)
        wgu = sb("wgu", NE * 2 * EF)
        wdn = sb("wdn", NE * D)
        vec = sb("vec", len(VEC))
        ident = sb("ident", P)
        ones_b = sb("ones_b", P, BF16)
        tri_b = sb("tri_b", P, BF16)
        decay1 = sb("decay1", 1)
        decay = sb("decay", T)
        zero_t = sb("zero_t", T)
        half4 = sb("half4", G)
        rev = sb("rev", (G, NE))
        region = sb("region", NE)
        region0 = sb("region0", NE)
        idf = sb("idf", G)
        filler = sb("filler", ROW)
        slot_no = sb("slot_no", NS)
        slot_i = sb("slot_i", NS, I32)
        id_i = sb("id_i", G, I32)
        one16 = sb("one16", NE)
        osum = two("osum", (G, NE), BF16)

        def W(name, f=0):
            at = MAIN[name][0] + f * P
            return wm[:, at:at + min(P, MAIN[name][1])]

        def V(name):
            return vec[:, VEC[name]:VEC[name] + 1]

        xin, xlate, xn0, xn1tok, xn1T = (two(n) for n in ("xin", "xlate", "xn0", "xn1tok", "xn1T"))
        stA, mvA, smA = two("stA", (G, 6)), two("mvA", (G, 2)), two("smA", (8, G))
        ew, z, q, er, rv, num, denp = (one(n) for n in ("ew", "z", "q", "er", "rv", "num", "denp"))
        e, ev, den, rq, p = (two(n) for n in ("e", "ev", "den", "rq", "p"))
        a, xa, an, xn2T = (two(n) for n in ("a", "xa", "an", "xn2T"))
        stC, mvC, smC = two("stC", (G, 6)), two("mvC", (G, 2)), two("smC", (2, G))
        kr = [sb(f"kr{f}", T) for f in range(F // P)]
        k2 = [sb(f"k2{f}", T) for f in range(F // P)]
        th, x2 = one("th"), two("x2")
        stE, mvE, smE = two("stE", (G, 6)), two("mvE", (G, 2)), two("smE", (2, G))
        h, hT = two("h"), two("hT")
        mx, ths, sc, cm = two("mx", G), two("ths", G), two("sc", G), two("cm", G)
        oh0, cand = two("oh0", (G, NE)), two("cand", (G, NE))
        oh = two("oh", (G, NE), BF16)
        prk, pmk = two("prk", (G, NE)), two("pmk", (G, NE))
        posf, posi = two("posf", G), two("posi", G, I32)
        sg = [sb(f"sg{f}", T) for f in range(SF // P)]
        act = [sb(f"act{f}", T) for f in range(SF // P)]
        dn = two("dn")
        rows = two("rows", (G, ROW))
        cnt_f, cnt_i, nsl_i, nsl, cum = sb("cnt_f", NE), sb("cnt_i", NE, I32), sb("nsl_i", NE, I32), sb("nsl", NE), sb("cum", NE)
        past, pastn = sb("past", (NS, NE)), sb("pastn", (NS, NE))
        eidf, firstf, rowf = sb("eidf", NS), sb("firstf", NS), sb("rowf", NS)
        eidc, place16, eidp, word = (sb(n, (WORDS, PACK)) for n in ("eidc", "place16", "eidp", "word"))
        row2f, row3f = sb("row2f", NS), sb("row3f", NS)
        eid_i, row_i, tail_i = sb("eid_i", WORDS, I32), sb("row_i", NS, I32), sb("tail_i", NE, I32)
        xrow = [rows[i // G][:, i % G, :] for i in range(2 * G)] + [b[:, 0:ROW] for b in kr + k2]
        xy = [b[:, j * (D + 1):(j + 1) * (D + 1)] for b in act + sg for j in range(2)]
        xhT, xsg, xact, xaT = (two(n, P) for n in ("xhT", "xsg", "xact", "xaT"))

        bank = [ctx.enter_context(nc.psum_tensor(f"bank{i}", [P, T], FP32)) for i in range(8)]
        ACC, SMALL = bank[0], bank[1]
        GU_BANK = [(bank[2], bank[3]), (bank[4], bank[5])]
        KE_BANK = [bank[2], bank[3], bank[4], bank[5]]
        REC_B, W_B, K_B, R_B, V_B = bank[2], bank[3], bank[4], bank[2], bank[5]
        T4_B, T5_B, T1_B, TM_B, T2_B, T3_B = bank[6], bank[6], bank[6], bank[7], bank[7], bank[7]
        RANK0 = G * NE
        LG = SMALL[:, 0:RANK0].rearrange("p (g e) -> p g e", e=NE)
        RK = SMALL[:, RANK0:2 * RANK0].rearrange("p (g e) -> p g e", e=NE)
        TOT = SMALL[:, 2 * RANK0:2 * RANK0 + NE]

        block = ctx.enter_context(nc.Block())

        def grp(tile, g):
            return tile[:, g * P:(g + 1) * P]

        LAST = 6
        FIRST_FULL = LAST + 2
        PAIRS = (NT - FIRST_FULL) // 2
        BODY_END = FIRST_FULL + 2 * PAIRS

        TAB_STEPS = 18

        def rounds(eng, one_round):
            for n in range(FIRST_FULL):
                one_round(n, n % 2)
            with eng.Fori(0, PAIRS) as i:
                for j in range(2):
                    one_round(InLoop(i, 2, FIRST_FULL + j), (FIRST_FULL + j) % 2)
            for n in range(BODY_END, NT + LAST):
                one_round(n, n % 2)

        def tiles(n, parity, behind):
            if isinstance(n, int) and not 0 <= n - behind < NT:
                return []
            return [(n - behind, (parity + behind) % 2)]

        SKEW = 7
        GATE_UP, ACT_T, DOWN = 2, 4, 6
        X_FIRST = 2 * RING
        X_LAPS = (NS - X_FIRST) // RING

        def slots_loop(eng, one_turn):
            for n in range(X_FIRST):
                one_turn(n, n % RING)
            with eng.Fori(0, X_LAPS) as i:
                for j in range(RING):
                    one_turn(InLoop(i, RING, X_FIRST + j), (X_FIRST + j) % RING)
            for n in range(X_FIRST + RING * X_LAPS, NS + SKEW):
                one_turn(n, n % RING)

        def slots(n, r, behind):
            if isinstance(n, int) and not 0 <= n - behind < NS:
                return []
            return [(n - behind, (r - behind) % RING)]

        def in16(t, par):
            return lap(t, 2, 16, 16)

        def wait_scattered(eng, t, par):
            if isinstance(t, int) and t < 0:
                return
            n_dma = 16 * G
            hold(eng, f"scat{par}", lap(t, 2, n_dma, n_dma))

        def wait_stored(eng, k, i):
            if isinstance(k, int) and k < 0:
                return
            hold(eng, f"xout{i}", lap(k, RING, 16, 16))

        LOADED = 8

        def entries(engine, table, at, most, count=LOADED):
            return nc.values_load_multi_w_load_instructions(
                table[0:1, bass.ds(at, count)], engines=[engine], min_val=0, max_val=most)[1]

        @block.sync
        def _(sp):
            sp.dma_start(vec[:, :], vecs).then_inc(s["v_in"], 16)
            cut = MAIN["Wkey"][0]
            cut2 = MAIN["router"][0]

            def load_x(t, par):
                wait(sp, "xn0", t - 2)
                wait(sp, "xn1tok", t - 2)
                sp.dma_start(xin[par][:, :].rearrange("p (g d) -> p g d", g=G), x_tile(t)).then_inc(s[f"x_in{par}"], 16)

            def load_x_late(t, par):
                wait(sp, "xa", t - 2)
                sp.dma_start(xlate[par][:, :].rearrange("p (g d) -> p g d", g=G), x_tile(t)).then_inc(s[f"xl_in{par}"], 16)

            def x_tile(t):
                if isinstance(t, int):
                    return x_tiles[t]
                return x_tiles[bass.ds(times(t, 1), 1)].rearrange("o p g d -> (o p) g d")

            def one_round(n, parity):
                for t, par in tiles(n, parity, 0):
                    load_x(t, par)
                if isinstance(n, int) and n == 0:
                    sp.dma_start(wm[:, 0:cut], w_main[:, 0:cut]).then_inc(s["w_in0"], 16)
                    sp.dma_start(wm[:, cut:cut2], w_main[:, cut:cut2]).then_inc(s["w_in1"], 16)
                    sp.dma_start(wm[:, cut2:], w_main[:, cut2:]).then_inc(s["w_in2"], 16)
                for t, par in tiles(n, parity, 1):
                    load_x_late(t, par)
                if isinstance(n, int) and n == 3:
                    sp.dma_start(wgu[:, :], w_gu).then_inc(s["w_in2"], 16)
                    sp.dma_start(wdn[:, :], w_down).then_inc(s["w_in2"], 16)
                    wait_filler(sp)
                    sp.dma_start(sorted_ap[FILL_ROW:FILL_ROW + P, :], filler[:, :]).then_inc(s["fill_out"], 16)

            def wait_filler(eng):
                eng.wait_ge(s["const_d"], 10)

            rounds(sp, one_round)

            sp.wait_ge(s["tab"], 1)
            for at in range(0, NE, LOADED):
                for row in entries(SP_ENGINE, tail_i, at, FILL_ROW - P):
                    sp.dma_start(sorted_ap[bass.ds(row, P), :], filler[:, :]).then_inc(s["fill_out"], 16)
            sp.wait_ge(s["fill_out"], 16 * (NE + 1))
            sp.wait_ge(s["tab"], TAB_STEPS)
            sp.wait_ge(s["scat0"], 16 * G * (NT // 2))
            sp.wait_ge(s["scat1"], 16 * G * (NT // 2))

            first_rows = []

            def one_turn(n, r):
                for k, i in slots(n, r, 0):
                    if i % LOADED == 0:
                        first_rows[:] = entries(SP_ENGINE, row_i, times(k, 1), FILL_ROW)
                    wait(sp, "xy", k - RING)
                    sp.dma_start(xrow[i], sorted_ap[bass.ds(first_rows[i % LOADED], P), :]).then_inc(s[f"xr_in{i}"], 16)

            slots_loop(sp, one_turn)

        @block.tensor
        def _(pe):
            mm = nc.tensor.matmul

            def transposes(dst, src, done):
                for g in range(G):
                    ins = nc.tensor.transpose(grp(dst, g), grp(src, g), ident[:, :])
                ins.then_inc(s[done], 1)

            def round_(n, parity):
                fs, es, ds_, cs, bs, as_ = (tiles(n, parity, k) for k in (5, 4, 3, 2, 1, 0))

                def gate_up(f):
                    for t, par in fs:
                        gb, ub = GU_BANK[f % 2]
                        if f == 0:
                            wait(pe, "hT", t)
                            pe.wait_ge(s["w_in2"], 16 * 3) if isinstance(n, int) and t == 0 else None
                            wait(pe, "E", t + 3)
                            wait(pe, "ew", t + 3)
                            if isinstance(t, int) and t + 3 >= NT:
                                wait(pe, "kr", t + 1)
                                wait(pe, "th", t + 1)
                        elif f == 1:
                            wait(pe, "z", t + 3)
                        else:
                            wait(pe, "sg", t, f - 1)
                        mm(gb[:, :], W("gate", f), hT[par][:, :], start=True, stop=True).then_inc(s["Gp"], 1)
                        if f == 1:
                            wait(pe, "ev", t + 3)
                        elif f > 1:
                            wait(pe, "act", t, f - 1)
                        mm(ub[:, :], W("up", f), hT[par][:, :], start=True, stop=True).then_inc(s["Up"], 1)

                def down(f):
                    for t, par in fs:
                        if f == 0:
                            wait(pe, "rv", t + 1)
                        wait(pe, "act", t, f + 1)
                        ins = mm(ACC[:, :], W("down", f), act[f][:, :], start=(f == 0), stop=(f == SF // P - 1))
                        if f == SF // P - 1:
                            ins.then_inc(s["DN"], 1)

                def key(f):
                    for t, par in ds_:
                        if f == 0:
                            wait(pe, "xn2T", t)
                            pe.wait_ge(s["w_in1"], 16) if isinstance(n, int) and t == 0 else None
                            wait(pe, "sg", t - 2)
                            wait(pe, "act", t - 2)
                            if not fs:
                                wait(pe, "E", t + 1)
                                wait(pe, "z", t + 1)
                                wait(pe, "ev", t + 1)
                        mm(KE_BANK[f][:, :], W("Wkey", f), xn2T[par][:, :], start=True, stop=True).then_inc(s["KE"], 1)

                gate_up(0)
                gate_up(1)
                down(0)
                gate_up(2)
                down(1)
                gate_up(3)
                down(2)
                for t, par in es:
                    wait(pe, "h", t)
                    wait(pe, "xn1T", t + 3)
                    transposes(T4_B, h[par], "T4")
                down(3)
                key(0)
                key(1)
                for t, par in cs:
                    wait(pe, "x2", t - 2)
                    for g in range(G):
                        wait(pe, "p", t, g + 1)
                        ins = mm(grp(TM_B, g), grp(p[par], g), W("Wo"), start=True, stop=True)
                    ins.then_inc(s["TM"], 1)
                for t, par in es:
                    wait(pe, "hT", t)
                    wait(pe, "rank", t - 1)
                    pe.wait_ge(s["w_in2"], 16) if isinstance(n, int) and t == 0 else None
                    for g in range(G):
                        ins = mm(LG[:, g, :], grp(hT[par], g), W("router"), start=True, stop=True)
                    ins.then_inc(s["LG"], 1)
                key(2)
                key(3)
                for t, par in ds_:
                    wait(pe, "kr", t, 1)
                    mm(REC_B[:, :], W("Wrec"), xn2T[par][:, :], start=True, stop=True).then_inc(s["REC"], 1)
                for t, par in fs:
                    wait(pe, "dn", t)
                    wait(pe, "hT", t + 1)
                    transposes(T5_B, dn[par], "T5")
                for t, par in ds_:
                    wait(pe, "dn", t - 2)
                    for f in range(F // P):
                        wait(pe, "k2", t, f + 1)
                        ins = mm(ACC[:, :], W("Wval", f), k2[f][:, :], start=(f == 0), stop=(f == F // P - 1))
                    ins.then_inc(s["VAL"], 1)
                for t, par in es:
                    wait(pe, "OS", t)
                    wait(pe, "route", t)
                    for g in range(G):
                        mm(RK[:, g, :], tri_b[:, :], oh[par][:, g, :], start=True, stop=(g == 0))
                        if g:
                            mm(RK[:, g, :], ones_b[:, :], osum[par][:, g - 1, :], start=False, stop=True)
                    mm(TOT, ones_b[:, :], osum[par][:, G - 1, :], start=True, stop=True).then_inc(s["RK"], 1)
                for t, par in bs:
                    wait(pe, "xn1T", t)
                    if isinstance(n, int) and t == 0:
                        pe.wait_ge(s["w_in0"], 16)
                    if ds_:
                        wait(pe, "kr", t - 2)
                    else:
                        wait(pe, "ew", t - 1)
                        wait(pe, "z", t - 1)
                    mm(W_B[:, :], W("Ww"), xn1T[par][:, :], start=True, stop=True).then_inc(s["Wp"], 1)
                    mm(K_B[:, :], W("Wk"), xn1T[par][:, :], start=True, stop=True).then_inc(s["Kp"], 1)
                for t, par in cs:
                    wait(pe, "an", t)
                    wait(pe, "a", t)
                    transposes(T2_B, an[par], "T2")
                for t, par in as_:
                    wait(pe, "xn1tok", t)
                    if isinstance(n, int) and t == 0:
                        pe.wait_ge(s["const_p"], 6)
                    if fs:
                        wait(pe, "base", t - 5)
                    wait(pe, "xn1T", t - 1)
                    if es:
                        wait(pe, "hT", t - 4)
                    transposes(T1_B, xn1tok[par], "T1")
                for t, par in bs:
                    if ds_:
                        wait(pe, "th", t - 2)
                    else:
                        wait(pe, "E", t - 1)
                    mm(R_B[:, :], W("Wr"), xn1T[par][:, :], start=True, stop=True).then_inc(s["Rp"], 1)
                    wait(pe, "ev", t - 1)
                    mm(V_B[:, :], W("Wv"), xn1T[par][:, :], start=True, stop=True).then_inc(s["Vp"], 1)
                for t, par in ds_:
                    wait(pe, "rv", t)
                    wait(pe, "xn2T", t + 1)
                    transposes(T3_B, rv[par], "T3")

            rounds(pe, lambda n, parity: round_(n, parity))

            pe.wait_ge(s["tab"], TAB_STEPS)
            pe.wait_ge(s["w_in2"], 48)

            words = []

            def expert(r, behind):
                place = r % LOADED + EID_PAD - behind
                return (words[place // PACK] >> (place % PACK * 4)) & (NE - 1)

            def one_turn(n, r):
                if r % LOADED == 0:
                    words[:] = entries(PE_ENGINE, eid_i, lap(n, PACK, 1), NE ** PACK - 1, LOADED // PACK + 1)
                for k, i in slots(n, r, DOWN):
                    wait(pe, "xaT", k)
                    wait(pe, "xy", k - 2)
                    mm(bank[6 + i % 2][:, 0:D], xaT[i % 2][:, :], wdn[:, bass.ds(expert(r, DOWN) * D, D)],
                       start=True, stop=True).then_inc(s["xDN"], 1)
                for k, i in slots(n, r, ACT_T):
                    wait(pe, "xact", k)
                    nc.tensor.transpose(bank[4 + i % 2][:, 0:P], xact[i % 2][:, :], ident[:, :]).then_inc(s["xT7"], 1)
                for k, i in slots(n, r, GATE_UP):
                    wait(pe, "xhT", k)
                    mm(bank[2 + i % 2][:, 0:2 * EF], xhT[i % 2][:, :], wgu[:, bass.ds(expert(r, GATE_UP) * (2 * EF), 2 * EF)],
                       start=True, stop=True).then_inc(s["xGU"], 1)
                for k, i in slots(n, r, 0):
                    pe.wait_ge(s[f"xr_in{i}"], lap(k, RING, 16, 16))
                    nc.tensor.transpose(bank[0 + i % 2][:, 0:P], xrow[i][:, 0:D], ident[:, :]).then_inc(s["xT6"], 1)

            slots_loop(pe, one_turn)

        @block.scalar
        def _(act_e):
            af = nc.scalar.activation
            act_e.wait_ge(s["v_in"], 16)
            af(decay1[:, :], V("decay"), ACT.Exp).then_inc(s["decay_s"], 1)

            def one_round(n, parity):
                fs, es, ds_, cs, bs, as_ = (tiles(n, parity, k) for k in (5, 4, 3, 2, 1, 0))

                def silu(f):
                    for t, par in fs:
                        wait(act_e, "Gp", t, f + 1)
                        wait(act_e, "act", t - 1, f + 1)
                        af(sg[f][:, :], GU_BANK[f % 2][0][:, :], ACT.Silu).then_inc(s["sg"], 1)

                def relu(f):
                    for t, par in ds_:
                        wait(act_e, "KE", t, f + 1)
                        wait(act_e, "k2", t - 1, f + 1)
                        af(kr[f][:, :], KE_BANK[f][:, :], ACT.Relu).then_inc(s["kr"], 1)

                def square(f):
                    for t, par in ds_:
                        wait(act_e, "kr", t, f + 1)
                        if f == 0:
                            wait(act_e, "VAL", t - 1)
                        af(k2[f][:, :], kr[f][:, :], ACT.Square).then_inc(s["k2"], 1)

                silu(0)
                silu(1)
                silu(2)
                silu(3)
                for t, par in es:
                    wait(act_e, "T4", t)
                    wait(act_e, "Up", t - 2)
                    af(hT[par][:, :], T4_B[:, :], ACT.Copy).then_inc(s["hT"], 1)
                for t, par in fs:
                    wait(act_e, "DN", t)
                    wait(act_e, "T5", t - 2)
                    af(dn[par][:, :], ACC[:, :], ACT.Copy).then_inc(s["dn"], 1)
                relu(0)
                relu(1)
                square(0)
                square(1)
                for t, par in es:
                    wait(act_e, "route", t, 1)
                    wait(act_e, "sc", t - 2)
                    af(ths[par][:, :], mx[par][:, :], ACT.Tanh, scale=0.5).then_inc(s["ths"], 1)
                relu(2)
                square(2)
                relu(3)
                square(3)
                for t, par in ds_:
                    wait(act_e, "REC", t)
                    wait(act_e, "rv", t - 1)
                    af(th[par][:, :], REC_B[:, :], ACT.Tanh, scale=0.5).then_inc(s["th"], 1)
                if bs:
                    nc.scalar.preload_act_table(ACT.Exp)
                for t, par in bs:
                    wait(act_e, "Wp", t)
                    wait(act_e, "z", t - 1)
                    af(ew[par][:, :], W_B[:, :], ACT.Exp).then_inc(s["ew"], 1)
                for t, par in cs:
                    wait(act_e, "T2", t)
                    wait(act_e, "REC", t - 2)
                    af(xn2T[par][:, :], T2_B[:, :], ACT.Identity, bias=V("b2"), scale=V("g2")).then_inc(s["xn2T"], 1)
                for t, par in as_:
                    wait(act_e, "T1", t)
                    wait(act_e, "Vp", t - 2)
                    af(xn1T[par][:, :], T1_B[:, :], ACT.Identity, bias=V("b1"), scale=V("g1")).then_inc(s["xn1T"], 1)
                for t, par in bs:
                    wait(act_e, "z", t)
                    wait(act_e, "den", t - 2)
                    wait(act_e, "ev", t - 2)
                    af(e[par][:, :], z[par][:, :], ACT.Exp).then_inc(s["e"], 1)
                    wait(act_e, "Rp", t)
                    wait(act_e, "q", t - 1)
                    af(er[par][:, :], R_B[:, :], ACT.Exp, scale=-1.0).then_inc(s["E"], 1)

            rounds(act_e, one_round)

            def one_turn(n, r):
                for k, i in slots(n, r, GATE_UP):
                    wait(act_e, "xGU", k)
                    wait(act_e, "xact", k - 2)
                    af(xsg[i % 2][:, :], bank[2 + i % 2][:, 0:EF], ACT.Silu).then_inc(s["xsg"], 1)
                for k, i in slots(n, r, 0):
                    wait(act_e, "xT6", k)
                    af(xhT[i % 2][:, :], bank[0 + i % 2][:, 0:P], ACT.Copy).then_inc(s["xhT"], 1)

            slots_loop(act_e, one_turn)

        @block.vector
        def _(dve):
            v = nc.vector
            nconst = [0]

            def const(ins):
                nconst[0] += 1
                ins.then_inc(s["const_d"], 1)
                dve.wait_ge(s["const_d"], nconst[0])

            const(v.memset(zero_t[:, :], 0.0))
            const(v.memset(half4[:, :], -0.5))
            for j in range(PACK):
                v.memset(place16[:, :, j], float(NE ** j))
            const(v.memset(eidc[:, :, :], 0.0))
            const(v.memset(filler[:, :], 0.0))
            const(v.memset(filler[:, 2 * D:ROW].bitcast(I32), NO_TOKEN))
            dve.wait_ge(s["const_p"], 6)
            const(v.tensor_scalar(region0[:, :], slot_no[:, 0:NE], float(REGION), None, ALU.mult))
            const(v.tensor_copy(region[:, :], region0[:, :]))
            for g in range(G):
                ins = v.tensor_scalar(rev[:, g, :], slot_no[:, 0:NE], -1.0, float(NE), ALU.mult, ALU.add)
            const(ins)
            dve.wait_ge(s["decay_s"], 1)
            const(v.tensor_scalar(decay[:, :], zero_t[:, :], decay1[:, 0:1], None, ALU.add))
            const(v.tensor_copy(ones_b[:, :], ones_b[:, :]))

            def stats(src, st, mv, stat_done, mv_done, t, pool_done):
                wait(dve, mv_done, t - 1)
                for g in range(G):
                    ins = v.bn_stats(st[:, g, :], grp(src, g))
                ins.then_inc(s[stat_done], 1)
                wait(dve, pool_done, t - 2)
                wait(dve, stat_done, t)
                stand_alone(dve)
                for g in range(G):
                    ins = v.bn_aggr(mv[:, g, :], st[:, g, :])
                ins.then_inc(s[mv_done], 1)

            def normed(dst, src, mv, rs, done):
                for g in range(G):
                    ins = v.tensor_scalar(grp(dst, g), grp(src, g), mv[:, g, 0:1], rs[:, g:g + 1],
                                          ALU.subtract, ALU.mult)
                ins.then_inc(s[done], 1)

            ntab = [0]

            def tab(ins):
                ntab[0] += 1
                ins.then_inc(s["tab"], 1)
                dve.wait_ge(s["tab"], ntab[0])

            def over_slots(ap):
                return ap.unsqueeze(1).to_broadcast([P, NS, NE])

            def tables(part):
                if part == 0:
                    wait(dve, "rank", NT - 1)
                    tab(v.tensor_copy(tail_i[:, :], region[:, :]))
                    tab(v.tensor_tensor(cnt_f[:, :], region[:, :], region0[:, :], ALU.subtract))
                    tab(v.tensor_scalar(cnt_i[:, :], cnt_f[:, :], float(P - 1), None, ALU.add))
                    tab(v.tensor_scalar(nsl_i[:, :], cnt_i[:, :], P.bit_length() - 1, None, ALU.logical_shift_right))
                    tab(v.tensor_copy(nsl[:, :], nsl_i[:, :]))
                    tab(v.tensor_tensor_scan(cum[:, :], one16[:, :], nsl[:, :], 0.0, ALU.mult, ALU.add))
                elif part == 1:
                    tab(v.tensor_tensor(past[:, :, :], over_slots(cum[:, :]),
                                        slot_no[:, :].unsqueeze(2).to_broadcast([P, NS, NE]), ALU.is_le))
                elif part == 2:
                    tab(v.tensor_tensor(pastn[:, :, :], past[:, :, :], over_slots(nsl[:, :]), ALU.mult))
                elif part == 3:
                    tab(v.reduce_sum(eidf[:, :], past[:, :, :], AX))
                else:
                    tab(v.reduce_sum(firstf[:, :], pastn[:, :, :], AX))
                    tab(v.tensor_scalar(rowf[:, :], eidf[:, :], float(REGION), None, ALU.mult))
                    tab(v.tensor_tensor(row2f[:, :], slot_no[:, :], firstf[:, :], ALU.subtract))
                    tab(v.scalar_tensor_tensor(row3f[:, :], row2f[:, :], float(P), rowf[:, :], ALU.mult, ALU.add))
                    tab(v.tensor_scalar(row_i[:, :], row3f[:, :], float(FILL_ROW), None, ALU.min))
                    tab(v.tensor_scalar(eidc[:, :, :].rearrange("p w k -> p (w k)")[:, EID_PAD:EID_PAD + NS], eidf[:, :],
                                        float(NE - 1), None, ALU.min))
                    tab(v.tensor_tensor(eidp[:, :, :], eidc[:, :, :], place16[:, :, :], ALU.mult))
                    tab(v.reduce_sum(word[:, :, 0], eidp[:, :, :], AX))
                    tab(v.tensor_copy(eid_i[:, :], word[:, :, 0]))
                    assert ntab[0] == TAB_STEPS

            def one_round(n, parity):
                fs, es, ds_, cs, bs, as_ = (tiles(n, parity, k) for k in (5, 4, 3, 2, 1, 0))

                def gated(f):
                    for t, par in fs:
                        wait(dve, "sg", t, f + 1)
                        wait(dve, "Up", t, f + 1)
                        if f == 0:
                            wait(dve, "DN", t - 1)
                        v.tensor_tensor(act[f][:, :], sg[f][:, :], GU_BANK[f % 2][1][:, :], ALU.mult).then_inc(s["act"], 1)

                def recip(part):
                    for t, par in cs:
                        c = slice(part * T // 4, (part + 1) * T // 4)
                        if part == 0:
                            wait(dve, "denp", t)
                            wait(dve, "E", t)
                            wait(dve, "rq", t - 1)
                            v.scalar_tensor_tensor(q[par][:, :], er[par][:, :], 1.0, denp[par][:, :], ALU.add,
                                                   ALU.mult).then_inc(s["q"], 1)
                            wait(dve, "q", t)
                        v.reciprocal(rq[par][:, c], q[par][:, c]).then_inc(s["rq"], 1)

                for t, par in cs:
                    wait(dve, "e", t)
                    wait(dve, "Vp", t)
                    wait(dve, "num", t - 2)
                    v.tensor_tensor(ev[par][:, :], e[par][:, :], V_B[:, :], ALU.mult).then_inc(s["ev"], 1)
                for t, par in cs:
                    wait(dve, "denp", t - 2)
                    v.tensor_tensor_scan(den[par][:, :], decay[:, :], e[par][:, :], 0.0, ALU.mult, ALU.add).then_inc(s["den"], 1)
                for t, par in es:
                    wait(dve, "T3", t)
                    wait(dve, "xa", t)
                    wait(dve, "base", t - 2)
                    v.scalar_tensor_tensor(x2[par][:, :], T3_B[:, :], 0.5, xa[par][:, :], ALU.mult, ALU.add).then_inc(s["x2"], 1)

                in_gap = tables if isinstance(n, int) and n == NT + 4 else (lambda part: None)
                in_gap(0)
                gated(0)
                in_gap(1)
                for t, par in cs:
                    wait(dve, "ev", t)
                    wait(dve, "p", t - 1)
                    v.tensor_tensor_scan(num[par][:, :], decay[:, :], ev[par][:, :], 0.0, ALU.mult, ALU.add).then_inc(s["num"], 1)
                for t, par in es:
                    wait(dve, "x2", t)
                    stats(x2[par], stE[par], mvE[par], "statE", "mvE", t, "poolE")
                recip(0)
                gated(1)
                in_gap(2)
                recip(1)
                gated(2)
                in_gap(3)
                recip(2)
                for t, par in es:
                    wait(dve, "poolE", t)
                    wait(dve, "T4", t - 2)
                    wait(dve, "hs", t - 2)
                    normed(h[par], x2[par], mvE[par], smE[par][:, 1, :], "h")
                gated(3)
                recip(3)
                for t, par in as_:
                    dve.wait_ge(s[f"x_in{par}"], in16(t, par))
                    stats(xin[par], stA[par], mvA[par], "statA", "mvA", t, "poolA")
                for t, par in cs:
                    wait(dve, "TM", t)
                    wait(dve, "xn0", t)
                    wait(dve, "an", t - 2)
                    wait(dve, "xa", t - 2)
                    v.tensor_tensor(a[par][:, :], TM_B[:, :], xn0[par][:, :], ALU.add).then_inc(s["a"], 1)
                    wait(dve, "a", t)
                    stats(a[par], stC[par], mvC[par], "statC", "mvC", t, "poolC")
                for t, par in es:
                    wait(dve, "LG", t)
                    wait(dve, "ths", t - 2)
                    v.reduce_max(mx[par][:, :], LG, AX).then_inc(s["route"], 1)
                    wait(dve, "route", t, 1)
                    v.tensor_tensor(oh0[par][:, :, :], LG, mx[par][:, :].unsqueeze(2).to_broadcast([P, G, NE]),
                                    ALU.is_equal).then_inc(s["route"], 1)
                    wait(dve, "route", t, 2)
                    v.tensor_tensor(cand[par][:, :, :], oh0[par][:, :, :], rev[:, :, :], ALU.mult).then_inc(s["route"], 1)
                    wait(dve, "route", t, 3)
                    v.reduce_max(cm[par][:, :], cand[par][:, :, :], AX).then_inc(s["route"], 1)
                    wait(dve, "route", t, 4)
                    wait(dve, "RK", t - 2)
                    v.tensor_tensor(oh[par][:, :, :], cand[par][:, :, :],
                                    cm[par][:, :].unsqueeze(2).to_broadcast([P, G, NE]), ALU.is_equal).then_inc(s["route"], 1)
                    wait(dve, "route", t, 5)
                    v.tensor_copy(osum[par][:, 0, :], oh[par][:, 0, :])
                    v.tensor_tensor(osum[par][:, 1, :], oh[par][:, 0, :], oh[par][:, 1, :], ALU.add).then_inc(s["OS"], 1)
                    wait(dve, "OS", t, 1)
                    v.tensor_tensor(osum[par][:, 2, :], osum[par][:, 1, :], oh[par][:, 2, :], ALU.add).then_inc(s["OS"], 1)
                    wait(dve, "OS", t, 2)
                    v.tensor_tensor(osum[par][:, 3, :], osum[par][:, 2, :], oh[par][:, 3, :], ALU.add).then_inc(s["OS"], 1)
                for t, par in fs:
                    wait(dve, "T5", t)
                    wait_scattered(dve, t - 2, par)
                    r3 = rows[par][:, :, D:2 * D]
                    v.tensor_tensor(r3, T5_B[:, :].rearrange("p (g d) -> p g d", g=G),
                                    x2[par][:, :].rearrange("p (g d) -> p g d", g=G), ALU.add).then_inc(s["base"], 1)
                in_gap(4)
                for t, par in as_:
                    wait(dve, "poolA", t)
                    wait(dve, "T1", t - 2)
                    normed(xn1tok[par], xin[par], mvA[par], smA[par][:, 6, :], "xn1tok")
                for t, par in cs:
                    wait(dve, "poolC", t)
                    wait(dve, "T2", t - 2)
                    normed(an[par], a[par], mvC[par], smC[par][:, 1, :], "an")
                for t, par in ds_:
                    wait(dve, "VAL", t)
                    wait(dve, "th", t)
                    wait(dve, "T3", t - 1)
                    v.scalar_tensor_tensor(rv[par][:, :], th[par][:, :], 1.0, ACC[:, :], ALU.add, ALU.mult).then_inc(s["rv"], 1)
                for t, par in es:
                    wait(dve, "RK", t)
                    v.tensor_tensor(prk[par][:, :, :], RK, region[:, :].unsqueeze(1).to_broadcast([P, G, NE]),
                                    ALU.add).then_inc(s["rank"], 1)
                    wait(dve, "rank", t, 1)
                    v.tensor_tensor(region[:, :], TOT, region[:, :], ALU.add).then_inc(s["rank"], 1)
                    v.tensor_tensor(pmk[par][:, :, :], prk[par][:, :, :], oh[par][:, :, :], ALU.mult).then_inc(s["rank"], 1)
                    wait(dve, "rank", t, 3)
                    v.reduce_sum(posf[par][:, :], pmk[par][:, :, :], AX).then_inc(s["rank"], 1)
                    wait(dve, "rank", t, 4)
                    wait_scattered(dve, t - 2, par)
                    v.tensor_copy(posi[par][:, :], posf[par][:, :]).then_inc(s["rank"], 1)
                for t, par in bs:
                    wait(dve, "Kp", t)
                    wait(dve, "ew", t)
                    wait(dve, "e", t - 1)
                    v.tensor_tensor(z[par][:, :], K_B[:, :], ew[par][:, :], ALU.subtract).then_inc(s["z"], 1)

            rounds(dve, one_round)

            def one_turn(n, r):
                for k, i in slots(n, r, DOWN):
                    wait(dve, "xDN", k)
                    wait_stored(dve, k - RING, i)
                    v.tensor_copy(xy[i][:, D:D + 1].bitcast(I32), xrow[i][:, 2 * D:ROW].bitcast(I32))
                    v.tensor_tensor(xy[i][:, 0:D], bank[6 + i % 2][:, 0:D], xrow[i][:, D:2 * D],
                                    ALU.add).then_inc(s["xy"], 1)
                for k, i in slots(n, r, ACT_T):
                    wait(dve, "xT7", k)
                    v.tensor_copy(xaT[i % 2][:, :], bank[4 + i % 2][:, 0:P]).then_inc(s["xaT"], 1)
                for k, i in slots(n, r, GATE_UP):
                    wait(dve, "xsg", k)
                    v.tensor_tensor(xact[i % 2][:, :], xsg[i % 2][:, :], bank[2 + i % 2][:, EF:2 * EF],
                                    ALU.mult).then_inc(s["xact"], 1)

            slots_loop(dve, one_turn)

        @block.gpsimd
        def _(gp):
            g_ = nc.gpsimd
            np_ = [0]

            def const(ins):
                np_[0] += 1
                ins.then_inc(s["const_p"], 1)
                gp.wait_ge(s["const_p"], np_[0])

            g_.memset(ident[:, :], 0.0)
            g_.memset(ones_b[:, :], 1.0)
            const(g_.memset(one16[:, :], 1.0))
            const(g_.affine_select(out=ident[:, :], in_=ident[:, :], compare_op=ALU.not_equal, fill=1.0, base=0,
                                   pattern=[[-1, P]], channel_multiplier=1))
            const(g_.affine_select(out=tri_b[:, :], in_=ones_b[:, :], compare_op=ALU.is_gt, fill=0.0, base=0,
                                   pattern=[[1, P]], channel_multiplier=-1))
            const(g_.iota(slot_i[:, :], pattern=[[1, NS]], base=0, channel_multiplier=0))
            const(g_.iota(id_i[:, :], pattern=[[P, G]], base=-T, channel_multiplier=1))
            g_.tensor_copy(idf[:, :], id_i[:, :])
            const(g_.tensor_copy(slot_no[:, :], slot_i[:, :]))
            gp.wait_ge(s["const_d"], 10)

            def rstd(sm, mv, name, t):
                g_.tensor_scalar(sm[:, 0, :], mv[:, :, 1], 1.0, LN_EPS, ALU.mult, ALU.add).then_inc(s[name], 1)
                wait(gp, name, t, 1)
                g_.tensor_tensor(sm[:, 1, :], sm[:, 0, :], half4[:, :], ALU.pow).then_inc(s[name], 1)

            def one_round(n, parity):
                fs, es, ds_, cs, bs, as_ = (tiles(n, parity, k) for k in (5, 4, 3, 2, 1, 0))

                for t, par in cs:
                    wait(gp, "den", t)
                    wait(gp, "q", t - 1)
                    g_.tensor_scalar(denp[par][:, :], den[par][:, :], 1.0, WKV_EPS, ALU.mult, ALU.add).then_inc(s["denp"], 1)
                for t, par in es:
                    wait(gp, "mvE", t)
                    wait(gp, "h", t - 2)
                    rstd(smE[par], mvE[par], "poolE", t)
                for g in range(G):
                    c = slice(g * P, (g + 1) * P)
                    for t, par in cs:
                        if g == 0:
                            wait(gp, "num", t)
                            wait(gp, "TM", t - 2)
                        wait(gp, "rq", t, g + 1)
                        g_.tensor_tensor(p[par][:, c], num[par][:, c], rq[par][:, c], ALU.mult).then_inc(s["p"], 1)
                    for t, par in tiles(n, parity, 6):
                        if g == 0:
                            wait(gp, "base", t)
                            wait(gp, "hs", t)
                            wait(gp, "ids", t)
                            wait(gp, "rank", t)
                        g_.indirect_dma_start(
                            sorted_ap, bass.IndirectOffsetOnAxis(posi[par][:, g:g + 1].bitcast(U32), 0),
                            rows[par][:, g, :], None).then_inc(s[f"scat{par}"], 16)
                for t, par in as_:
                    sm = smA[par]
                    wait(gp, "mvA", t)
                    wait(gp, "xn1tok", t - 2)
                    wait(gp, "xn0", t - 2)
                    var = mvA[par][:, :, 1]
                    g_.tensor_scalar(sm[:, 5, :], mvA[par][:, :, 0], -1.0, 0.0, ALU.mult, ALU.add)
                    rstd(sm, mvA[par], "poolA", t)
                    wait(gp, "poolA", t, 2)
                    g_.tensor_tensor(sm[:, 2, :], sm[:, 1, :], sm[:, 1, :], ALU.mult).then_inc(s["poolA"], 1)
                    wait(gp, "poolA", t, 3)
                    g_.tensor_tensor(sm[:, 3, :], var, sm[:, 2, :], ALU.mult).then_inc(s["poolA"], 1)
                    wait(gp, "poolA", t, 4)
                    g_.tensor_scalar(sm[:, 4, :], sm[:, 3, :], 1.0, LN_EPS, ALU.mult, ALU.add).then_inc(s["poolA"], 1)
                    wait(gp, "poolA", t, 5)
                    g_.tensor_tensor(sm[:, 7, :], sm[:, 4, :], half4[:, :], ALU.pow).then_inc(s["poolA"], 1)
                    wait(gp, "poolA", t, 6)
                    g_.tensor_tensor(sm[:, 6, :], sm[:, 1, :], sm[:, 7, :], ALU.mult).then_inc(s["poolA"], 1)
                for t, par in cs:
                    wait(gp, "mvC", t)
                    wait(gp, "an", t - 2)
                    rstd(smC[par], mvC[par], "poolC", t)
                for t, par in as_:
                    sm = smA[par]
                    wait(gp, "a", t - 2)
                    for g in range(G):
                        ins = g_.tensor_scalar(grp(xn0[par], g), grp(xin[par], g), sm[:, 5, g:g + 1], sm[:, 1, g:g + 1],
                                               ALU.add, ALU.mult)
                    ins.then_inc(s["xn0"], 1)
                for t, par in es:
                    wait(gp, "ths", t)
                    g_.tensor_scalar(sc[par][:, :], ths[par][:, :], 0.5, 0.5, ALU.mult, ALU.add).then_inc(s["sc"], 1)
                for t, par in es:
                    wait(gp, "sc", t)
                    wait(gp, "h", t)
                    wait_scattered(gp, t - 2, par)
                    for g in range(G):
                        ins = g_.tensor_scalar(rows[par][:, g, 0:D], grp(h[par], g), sc[par][:, g:g + 1], 1.0,
                                               ALU.mult, ALU.mult)
                    ins.then_inc(s["hs"], 1)
                    wait(gp, "ids", t - 1)
                    g_.tensor_scalar(idf[:, :], idf[:, :], 1.0, float(T), ALU.mult, ALU.add).then_inc(s["ids"], 1)
                    wait(gp, "ids", t, 1)
                    g_.tensor_copy(rows[par][:, :, 2 * D:ROW].bitcast(I32),
                                   idf[:, :].unsqueeze(2)).then_inc(s["ids"], 1)
                for t, par in cs:
                    hold(gp, f"xl_in{par}", in16(t, par))
                    wait(gp, "a", t)
                    wait(gp, "x2", t - 2)
                    g_.tensor_tensor(xa[par][:, :], xlate[par][:, :], a[par][:, :], ALU.add).then_inc(s["xa"], 1)

            rounds(gp, one_round)

            def one_turn(n, r):
                for k, i in slots(n, r, SKEW):
                    wait(gp, "xy", k)
                    g_.indirect_dma_start(
                        out, bass.IndirectOffsetOnAxis(xy[i][:, D:D + 1].bitcast(U32), 0),
                        xy[i][:, 0:D], None, bounds_check=NTOK - 1, oob_is_err=False).then_inc(s[f"xout{i}"], 16)

            slots_loop(gp, one_turn)
            for i in range(RING):
                gp.wait_ge(s[f"xout{i}"], 16 * (NS // RING))


_OUTS = [((NTOK, D), "float32")]


def kernel(**inputs):
    import concourse.bacc as _bacc
    from concourse.bass_utils import run_bass_kernel_spmd as _run

    a = {k[3:]: np.asarray(v) for k, v in inputs.items()}

    def chunks(w):
        n = w.shape[0] // P
        return w.reshape(n, P, w.shape[1]).transpose(1, 0, 2).reshape(P, -1)

    main = {
        "Ww": a["attn_Ww"].T, "Wk": a["attn_Wk"].T, "Wr": a["attn_Wr"].T, "Wv": a["attn_Wv"].T, "Wo": a["attn_Wo"].T,
        "Wkey": a["attn_Wkey"].T, "Wrec": a["attn_Wrec"].T, "Wval": chunks(a["attn_Wval"].T),
        "router": a["ffn_router_w"].T, "gate": a["ffn_shared_gate_w"].T, "up": a["ffn_shared_up_w"].T,
        "down": chunks(a["ffn_shared_down_w"].T),
    }
    vec = (a["attn_ln1_g"], a["attn_ln1_b"], a["attn_ln2_g"], a["attn_ln2_b"], a["attn_time_decay"])
    arrays = {
        "x": a["attn_x"].reshape(NTOK, D),
        "w_main": np.concatenate([main[n] for n in MAIN], axis=1),
        "w_gu": a["ffn_gate_up_proj"].transpose(1, 0, 2).reshape(D, -1),
        "w_down": a["ffn_down_proj"].transpose(1, 0, 2).reshape(EF, -1),
        "vecs": np.stack(vec, axis=1),
    }
    arrays = {k: np.ascontiguousarray(v) for k, v in arrays.items()}
    nc = _bacc.Bacc("TRN2", target_bir_lowering=False, num_devices=1)
    args = [nc.dram_tensor(k, v.shape, mybir.dt.from_np(v.dtype), kind="ExternalInput").ap() for k, v in arrays.items()]
    args.append(nc.dram_tensor("out", (NTOK, D), FP32, kind="ExternalOutput").ap())
    program(nc, *args)
    r = _run(nc, [arrays], core_ids=[0])
    return r.results[0]["out"].reshape(B, S, D)
```
